# Optimizing a Trainium2 kernel written in Bass

```python
import numpy as np
import jax
import jax.numpy as jnp

def _softmax(x, axis=-1):
    return jax.nn.softmax(x, axis=axis)

def _gelu(x):
    return jax.nn.gelu(x, approximate=True)

def _silu(x):
    return jax.nn.silu(x)

def _sigmoid(x):
    return jax.nn.sigmoid(x)

def _layernorm(x, axis=-1, eps=1e-05):
    m = jnp.mean(x, axis=axis, keepdims=True)
    v = jnp.var(x, axis=axis, keepdims=True)
    return (x - m) / jnp.sqrt(v + eps)

def _scatter_add(tgt, idx, src, axis=0):
    return tgt.at[idx].add(src)

def _segment_sum(src, seg, n):
    return jax.ops.segment_sum(src, seg, n)
kernel_name = 'mk_gnn_ffn_d1_gnn_r8_5dd583'

def setup_inputs(seed: int=0):
    np.random.seed(seed)
    _w = jnp.asarray

    def _rec_inputs():
        import jax
        import jax.numpy as jnp
        _gk = jax.random.key(seed)
        x = -0.0003713 + 1 * jax.random.normal(jax.random.fold_in(_gk, 1), (6250, 256), jnp.float32)
        _s = jax.random.randint(jax.random.fold_in(_gk, 2), (100000,), 0, 6250, jnp.int32)
        _d = jax.random.randint(jax.random.fold_in(_gk, 3), (100000,), 0, 6250, jnp.int32)
        _loop = jnp.arange(6250, dtype=jnp.int32)
        src = jnp.concatenate([_s, _d, _loop])
        dst = jnp.concatenate([_d, _s, _loop])
        _o = jnp.argsort(dst, stable=True)
        src = src[_o]
        dst = dst[_o]
        edge_weight = jax.random.uniform(jax.random.fold_in(_gk, 12), (206250,), jnp.float32, 0.0, 1)
        return (x, src, dst, edge_weight)
    x, src, dst, edge_weight = _rec_inputs()

    def _L0_gnn_setup():
        import jax, jax.numpy as jnp
        import numpy as np
        N = 6250
        E = 200000
        D = 256
        K = 2

        def spmm(edge_row, edge_col, edge_val, feats):
            msgs = edge_val[:, None] * feats[edge_col]
            return jax.ops.segment_sum(msgs, edge_row, num_segments=N)
        key = jax.random.key(seed)
        k1, k2, k3, k4, k5 = jax.random.split(key, 5)
        x = jax.random.normal(k1, (N, D), dtype=jnp.float32)
        edge_row = jax.random.randint(k2, (E,), 0, N, dtype=jnp.int64)
        edge_col = jax.random.randint(k3, (E,), 0, N, dtype=jnp.int64)
        edge_val = jax.random.uniform(k4, (E,), dtype=jnp.float32)
        fan_in, fan_out = (D * (K + 1), D)
        std = np.sqrt(2.0) * np.sqrt(2.0 / (fan_in + fan_out))
        W = jax.random.normal(k5, (fan_in, fan_out), dtype=jnp.float32) * std
        b = jnp.zeros((fan_out,), dtype=jnp.float32)
        return {'x': x, 'edge_row': edge_row, 'edge_col': edge_col, 'edge_val': edge_val, 'W': W, 'b': b}
    _L0_gnn_all = _L0_gnn_setup()
    _L0_gnn_in = {k: v for k, v in _L0_gnn_all.items() if k in ('W', 'b')}
    del _L0_gnn_all

    def _L0_ffn_setup():
        import jax, jax.numpy as jnp
        import numpy as np
        E = 8
        K = 2
        D = 256
        H = 512
        DOUT = 256
        EPS = 1e-05
        key = jax.random.key(seed)
        ks = jax.random.split(key, 9)
        s = 0.02
        return {'x': jax.random.normal(ks[0], (4, 1024, D), jnp.float32), 'gamma': 1.0 + 0.05 * jax.random.normal(ks[1], (D,), jnp.float32), 'beta': 0.05 * jax.random.normal(ks[2], (D,), jnp.float32), 'Wr': 0.01 * jax.random.normal(ks[3], (D, E), jnp.float32), 'br': jnp.zeros((E,), jnp.float32), 'W1': s * jax.random.normal(ks[4], (E, D, H), jnp.float32), 'b1': s * jax.random.normal(ks[5], (E, H), jnp.float32), 'W2': s * jax.random.normal(ks[6], (E, H, DOUT), jnp.float32), 'b2': s * jax.random.normal(ks[7], (E, DOUT), jnp.float32)}
    _L0_ffn_all = _L0_ffn_setup()
    _L0_ffn_in = {k: v for k, v in _L0_ffn_all.items() if k in ('gamma', 'beta', 'Wr', 'br', 'W1', 'b1', 'W2', 'b2')}
    del _L0_ffn_all
    return {'x': x, 'src': src, 'dst': dst, 'edge_weight': edge_weight, 'L0_gnn_W': _L0_gnn_in['W'], 'L0_gnn_b': _L0_gnn_in['b'], 'L0_ffn_gamma': _L0_ffn_in['gamma'], 'L0_ffn_beta': _L0_ffn_in['beta'], 'L0_ffn_Wr': _L0_ffn_in['Wr'], 'L0_ffn_br': _L0_ffn_in['br'], 'L0_ffn_W1': _L0_ffn_in['W1'], 'L0_ffn_b1': _L0_ffn_in['b1'], 'L0_ffn_W2': _L0_ffn_in['W2'], 'L0_ffn_b2': _L0_ffn_in['b2']}

def reference(x, src, dst, edge_weight, L0_gnn_W, L0_gnn_b, L0_ffn_gamma, L0_ffn_beta, L0_ffn_Wr, L0_ffn_br, L0_ffn_W1, L0_ffn_b1, L0_ffn_W2, L0_ffn_b2):
    import jax
    import jax.numpy as jnp

    def _L0_gnn_ref(x, edge_row, edge_col, edge_val, W, b):
        import jax, jax.numpy as jnp
        import numpy as np
        N = 6250
        E = 200000
        D = 256
        K = 2

        def spmm(edge_row, edge_col, edge_val, feats):
            msgs = edge_val[:, None] * feats[edge_col]
            return jax.ops.segment_sum(msgs, edge_row, num_segments=N)
        fstack = [x]
        for _ in range(K):
            fstack.append(spmm(edge_row, edge_col, edge_val, fstack[-1]))
        h = jnp.concatenate(fstack, axis=-1)
        out = h @ W + b
        return out

    def _L0_ffn_ref(x, gamma, beta, Wr, br, W1, b1, W2, b2):
        import jax, jax.numpy as jnp
        import numpy as np
        E = 8
        K = 2
        D = 256
        H = 512
        DOUT = 256
        EPS = 1e-05
        mu = jnp.mean(x, axis=-1, keepdims=True)
        var = jnp.mean(jnp.square(x - mu), axis=-1, keepdims=True)
        xn = (x - mu) * jax.lax.rsqrt(var + EPS) * gamma + beta
        logits = jnp.einsum('bsd,de->bse', xn, Wr) + br
        top_vals, top_idx = jax.lax.top_k(logits, K)
        w = jax.nn.softmax(top_vals, axis=-1)
        w_full = jnp.einsum('bsk,bske->bse', w, jax.nn.one_hot(top_idx, E, dtype=w.dtype))
        y = jnp.zeros(x.shape[:-1] + (DOUT,), x.dtype)
        for e in range(E):
            h = jax.nn.gelu(jnp.einsum('bsd,dh->bsh', xn, W1[e]) + b1[e], approximate=False)
            y_e = jnp.einsum('bsh,hd->bsd', h, W2[e]) + b2[e]
            y = y + y_e * w_full[..., e, None]
        return y
    x = x + _L0_gnn_ref(_layernorm(x, axis=-1), src, dst, edge_weight, L0_gnn_W, L0_gnn_b)
    x = x + _L0_ffn_ref(_layernorm(x, axis=-1)[None], L0_ffn_gamma, L0_ffn_beta, L0_ffn_Wr, L0_ffn_br, L0_ffn_W1, L0_ffn_b1, L0_ffn_W2, L0_ffn_b2)[0]
    return x

_drawn_inputs = setup_inputs


def setup_inputs(seed=0):
    import zlib

    import numpy as np

    out = dict(_drawn_inputs(seed))
    spreads = {'L0_gnn_b': (0.0, 0.8), 'L0_ffn_br': (0.0, 0.8)}
    factors = {'L0_ffn_gamma': 8.0,
     'L0_ffn_beta': 8.0,
     'L0_ffn_Wr': 8.0,
     'L0_ffn_W1': 8.0,
     'L0_ffn_b1': 59.642,
     'L0_ffn_W2': 8.0,
     'L0_ffn_b2': 64.0}
    for name, (base, spread) in spreads.items():
        noise = np.random.default_rng([zlib.crc32(name.encode()), seed]).standard_normal(out[name].shape)
        drawn = base * np.exp(spread * noise) if base else spread * noise
        out[name] = jnp.asarray(drawn.astype(out[name].dtype))
    for name, factor in factors.items():
        out[name] = (out[name] * factor).astype(out[name].dtype)
    return out
```

```python
from contextlib import ExitStack

import concourse.bass as bass
from concourse import mybir

F32 = mybir.dt.float32
BF16 = mybir.dt.bfloat16
I32 = mybir.dt.int32
U32 = mybir.dt.uint32
ALU = mybir.AluOpType
ACT = mybir.ActivationFunctionType
AX = mybir.AxisListType.X
ds = bass.ds

P = 128
EPS = 1e-5

BUCKET = 32
CG = 8
WIN = 128
GPI = 2
RING = CG * GPI
LEAD = 5
SLACK = 1
SORT = 8
COUNT = 31


def wait_later(engine, sem, value):
    if not isinstance(value, int) or value > 0:
        engine.wait_ge(sem, value)


def build(nc, x, src, dst, edge_weight, gnn_W, gnn_b, gamma, beta, Wr, br, W1, b1, W2, b2, out):
    N, D = x.shape
    E = src.shape[0]
    NX, _, H = W1.shape
    DK = D // P
    HC = H // P
    B = 125
    NB = N // B
    assert N == NB * B and NB % 2 == 0 and DK == 2 and NX == 8

    chunks = -(-E // P)
    turns = -(-chunks // RING)
    groups = turns * GPI
    used = groups * CG
    count_turns = -(-chunks // COUNT)
    assert chunks == count_turns * COUNT and count_turns % 2 == 0
    last_full = E - (P - 1) * chunks
    assert 0 < last_full <= chunks
    BLO = 16
    BHI = -(-(-(-N // BUCKET)) // BLO)
    NBK = BHI * BLO
    assert NBK <= 256
    edge_steps = (turns - LEAD) // 2
    assert turns == LEAD + 2 * edge_steps and 3 < edge_steps < NB
    BG = 2 * GPI
    assert BG == 4
    group_sets = -(-groups // P)
    group_cols = group_sets * P

    ctx = ExitStack()

    def sb(name, shape, dt=F32):
        return ctx.enter_context(nc.sbuf_tensor(name, shape, dt))

    def ps(name, shape):
        return ctx.enter_context(nc.psum_tensor(name, shape, F32))

    def sem(name):
        return nc.alloc_semaphore(name)

    with ctx:
        xn0_rows = nc.dram_tensor("xn0_rows", (N, D), F32).ap()
        hop1_rows = nc.dram_tensor("hop1_rows", (N, D), F32).ap()
        y_rows = nc.dram_tensor("y_rows", (N, D), F32).ap()
        window_dram = nc.dram_tensor("window_dram", (2, group_cols), I32).ap()
        count_dram = nc.dram_tensor("count_dram", (BHI, BLO), F32).ap()
        sorted_edges = nc.dram_tensor("sorted_edges", (P * chunks, 4), F32).ap()

        accT = sb("accT", [P, DK, N + WIN])
        gatherT = sb("gatherT", [P, used])
        wT = sb("wT", [P, used])
        relT = sb("relT", [P, used])
        idx_stage = sb("idx_stage", [P, GPI, CG], I32)
        ring = sb("ring", [P, RING, D])
        onehot = sb("onehot", [P, GPI, CG, WIN])
        windowf = sb("windowf", [P, 2, group_cols])
        base_i = sb("base_i", [P, group_cols], I32)
        span = sb("span", [P, 4])
        rounds_i = sb("rounds_i", [1, 2], I32)
        due = sb("due", [1, group_cols])
        due_i = sb("due_i", [1, group_cols], I32)
        rounds_all = sb("rounds_all", [P, 2], I32)
        iota_i = sb("iota_i", [P, NBK], I32)
        iota = sb("iota", [P, NBK])
        iota_b = sb("iota_b", [P, NBK], BF16)
        ident = sb("ident", [P, P])
        ones = sb("ones", [1, P])
        eps = sb("eps", [P, 1])
        zeros = sb("zeros", [P, DK, B])
        W1s = sb("W1s", [P, NX, DK, H])
        W2s = sb("W2s", [P, NX, HC, D])
        Wg = sb("Wg", [P, 3 * DK, D])
        Wrs = sb("Wrs", [P, DK, NX])
        brs = sb("brs", [P, NX])
        bg = sb("bg", [1, D])
        b2s = sb("b2s", [NX, D])
        NV = NX * HC + 2 * DK
        vec_rows = sb("vec_rows", [NV, P])
        vecT = sb("vecT", [P, NV])
        node_mem = sb("node_mem", [P, 2 * HC * B + 4 * D])
        row_tile = sb("row_tile", [P, 4, D])
        colT = sb("colT", [P, 2, DK, B])
        stats = sb("stats", [P, 2, 6])
        mv = sb("mv", [P, 2, 2])
        sd = sb("sd", [P, 2])
        rstd = sb("rstd", [P, 2])

        pool_mem = accT[:, :, :].rearrange("p k n -> p (k n)")
        raw = pool_mem[:, 0:3 * chunks].rearrange("p (t c) -> p t c", t=3)
        raw_i = raw.bitcast(I32)
        buckets_i = pool_mem[:, 3 * chunks:4 * chunks].bitcast(I32)
        buckets = pool_mem[:, 4 * chunks:4 * chunks + chunks // 2].bitcast(BF16)
        digits_i = pool_mem[:, 5 * chunks:7 * chunks].rearrange("p (t c) -> p t c", t=2).bitcast(I32)
        back = pool_mem[:, 3 * chunks:7 * chunks].rearrange("p (c r) -> p c r", r=4)
        assert 7 * chunks <= DK * (N + WIN) and chunks % 2 == 0
        ring_mem = ring[:, :, :].rearrange("p s d -> p (s d)")
        taken = [0]

        def carve(columns):
            taken[0] += columns
            assert taken[0] <= RING * D
            return ring_mem[:, taken[0] - columns:taken[0]]
        ext_part = carve(2 * group_cols).rearrange("p (t g) -> p t g", t=2)
        window = node_mem[:, 0:2 * group_cols].bitcast(I32)\
            .rearrange("p (t g) -> p t g", t=2)
        group_ext = sb("group_ext", [P, 2, group_sets], I32)
        digit_hot = carve(COUNT * (BHI + BLO)).bitcast(BF16).rearrange("p (a c w) -> p a c w", a=2, c=COUNT)
        bucket_hot = carve(SORT * NBK).bitcast(BF16).rearrange("p (a c w) -> p a c w", a=2, c=SORT)
        before = sb("before", [P, P], BF16)
        not_before = sb("not_before", [P, P], BF16)
        all_ones = sb("all_ones", [P, P], BF16)
        tri = sb("tri", [P, P])
        hot_rank = carve(2 * NBK).rearrange("p (a w) -> p a w", a=2)
        rank_f = sb("rank_f", [P, 2, SORT])
        rank_i = sb("rank_i", [P, 3, 2, SORT], I32)
        row_idx = sb("row_idx", [P, 2, SORT], I32)
        record = sb("record", [P, 2, SORT, 4])
        counts = sb("counts", [BHI, BLO])
        count_row = sb("count_row", [1, 3, NBK])

        x_blk, row_blk, y_blk = node_mem[0:B, 0:D], row_tile[0:B, 0, :], row_tile[0:B, 1, :]
        hopT = sb("hopT", [P, 2, DK, B])
        xnT = colT
        gelu_out = node_mem[:, 0:2 * HC * B].rearrange("p (a c n) -> p a c n", a=2, c=HC)
        y_in = node_mem[:, 2 * HC * B:2 * HC * B + 2 * D].rearrange("p (a d) -> p a d", a=2)
        x1 = node_mem[:, 2 * HC * B + 2 * D:2 * HC * B + 4 * D].rearrange("p (a d) -> p a d", a=2)
        acc, z = row_tile[:, 0:2, :], row_tile[:, 2:4, :]
        small = sb("small", [P, 8, 8])
        logits, top8, top8f = small[:, 0, :], small[:, 1, :], small[:, 2, :]
        pick1, w_full, pair = small[:, 3, :], small[:, 4:6, :], small[:, 6, :]
        top_idx = sb("top_idx", [P, 8], U32)
        wfT = sb("wfT", [NX, B])

        bank = [ps(f"bank{i}", [P, 512]) for i in range(8)]

        loaded = [sem(f"loaded{i}") for i in range(3)]
        consts_loaded = sem("consts_loaded")
        weights_loaded = sem("weights_loaded")

        raw_padded, iota_made, iota_floated, ident_made, tri_made, tri_cast = (
            sem("raw_padded"), sem("iota_made"), sem("iota_floated"), sem("ident_made"), sem("tri_made"), sem("tri_cast"))
        consts_set, vec_turned = sem("consts_set"), sem("vec_turned")
        bucket_step, digits_hot, counted, counts_out = (sem("bucket_step"), sem("digits_hot"), sem("counted"),
                                                        sem("counts_out"))
        counts_stored, counts_back, count_step = sem("counts_stored"), sem("counts_back"), sem("count_step")

        with nc.Block() as block:
            @block.sync
            def _(sp):
                sp.wait_ge(raw_padded, 3)
                for n, arr in enumerate((src, dst, edge_weight)):
                    to = raw if n == 2 else raw_i
                    sp.dma_start(to[0:P - 1, n, :], arr[0:(P - 1) * chunks].rearrange("(p c) -> p c", c=chunks))\
                        .then_inc(loaded[n], 16)
                    sp.dma_start(to[P - 1:P, n, 0:last_full], arr[(P - 1) * chunks:E].rearrange("(p c) -> p c", p=1))\
                        .then_inc(loaded[n], 16)
                sp.wait_ge(counts_out, 1)
                sp.dma_start(count_dram, counts[:, :]).then_inc(counts_stored, 16)
                sp.wait_ge(counts_stored, 16)
                sp.dma_start(count_row[:, 0, :], count_dram.rearrange("h l -> (h l)").rearrange("(a n) -> a n", a=1))\
                    .then_inc(counts_back, 16)

            @block.scalar
            def _(act):
                act.dma_start(vec_rows[0:NX * HC, :], b1.rearrange("e (c p) -> (e c) p", p=P)).then_inc(consts_loaded, 16)
                act.dma_start(vec_rows[NX * HC:NX * HC + DK, :], gamma.rearrange("(k p) -> k p", p=P))\
                    .then_inc(consts_loaded, 16)
                act.dma_start(vec_rows[NX * HC + DK:NV, :], beta.rearrange("(k p) -> k p", p=P)).then_inc(consts_loaded, 16)
                act.dma_start(brs[:, :], br.partition_broadcast(P)).then_inc(consts_loaded, 16)
                act.dma_start(bg[:, :], gnn_b.rearrange("(a n) -> a n", a=1)).then_inc(consts_loaded, 16)
                act.dma_start(b2s[:, :], b2).then_inc(consts_loaded, 16)
                act.dma_start(Wrs[:, :, :], Wr.rearrange("(k p) e -> p k e", p=P)).then_inc(consts_loaded, 16)
                act.dma_start(Wg[:, :, :], gnn_W.rearrange("(j p) d -> p j d", p=P)).then_inc(consts_loaded, 16)

            @block.gpsimd
            def _(pool):
                pool.memset(raw_i[:, 0, last_full:chunks], N - 1).then_inc(raw_padded, 1)
                pool.memset(raw_i[:, 1, last_full:chunks], 0).then_inc(raw_padded, 1)
                pool.memset(raw[:, 2, last_full:chunks], 0.0).then_inc(raw_padded, 1)
                pool.iota(iota_i[:, :], pattern=[[1, NBK]], base=0, channel_multiplier=0).then_inc(iota_made, 1)
                pool.memset(ident[:, :], 0.0).then_inc(ident_made, 1)
                pool.memset(tri[:, :], 1.0).then_inc(tri_made, 1)
                pool.wait_ge(ident_made, 1)
                pool.affine_select(out=ident[:, :], in_=ident[:, :], compare_op=ALU.not_equal, fill=1.0,
                                   base=0, pattern=[[-1, P]], channel_multiplier=1).then_inc(ident_made, 1)
                pool.wait_ge(tri_made, 1)
                pool.affine_select(out=tri[:, :], in_=tri[:, :], compare_op=ALU.is_gt, fill=0.0,
                                   base=0, pattern=[[1, P]], channel_multiplier=-1).then_inc(tri_made, 1)
                pool.memset(ones[:, :], 1.0).then_inc(consts_set, 1)
                pool.memset(eps[:, :], EPS).then_inc(consts_set, 1)
                pool.memset(zeros[:, :, :], 0.0).then_inc(consts_set, 1)
                pool.memset(all_ones[:, :], 1.0).then_inc(consts_set, 1)
                pool.dma_start(W1s[:, :, :, :], W1.rearrange("e (k p) h -> p e k h", p=P)).then_inc(weights_loaded, 16)
                pool.dma_start(W2s[:, :, :, :], W2.rearrange("e (c p) d -> p e c d", p=P)).then_inc(weights_loaded, 16)

            @block.tensor
            def _(pe):
                def count(turn, a, first=False, final=False):
                    pe.wait_ge(digits_hot, turn + 1)
                    for c in range(COUNT):
                        last = pe.matmul(bank[6][0:BHI, 0:BLO], digit_hot[:, a, c, 0:BHI], digit_hot[:, a, c, BHI:BHI + BLO],
                                         start=(first and c == 0), stop=(final and c == COUNT - 1), skip_group_check=True)
                    last.then_inc(counted, 1)
                count(0, 0, first=True)
                count(1, 1)
                with pe.Fori(1, count_turns // 2 - 1) as m:
                    for a in range(2):
                        count(m * 2 + a, a)
                count(count_turns - 2, 0)
                count(count_turns - 1, 1, final=True)
                pe.wait_ge(ident_made, 2)
                pe.wait_ge(consts_loaded, 16 * 8)
                pe.transpose(bank[7][:, 0:NV], vec_rows[:, :], ident[0:NV, 0:NV]).then_inc(vec_turned, 1)

            @block.vector
            def _(dve):
                dve.wait_ge(iota_made, 1)
                dve.tensor_copy(iota[:, :], iota_i[:, :]).then_inc(iota_floated, 1)
                dve.wait_ge(iota_floated, 1)
                dve.tensor_copy(iota_b[:, :], iota[:, :]).then_inc(iota_floated, 1)
                dve.wait_ge(tri_made, 2)
                dve.tensor_copy(before[:, :], tri[:, :]).then_inc(tri_cast, 1)
                dve.tensor_scalar(not_before[:, :], tri[:, :], -1.0, 1.0, ALU.mult, ALU.add).then_inc(tri_cast, 1)
                dve.wait_ge(loaded[0], 32)
                dve.tensor_scalar(buckets_i, raw_i[:, 0, :], BUCKET.bit_length() - 1, None,
                                  ALU.logical_shift_right).then_inc(bucket_step, 1)
                dve.wait_ge(bucket_step, 1)
                dve.tensor_copy(buckets, buckets_i).then_inc(bucket_step, 1)
                dve.tensor_scalar(digits_i[:, 0, :], buckets_i, BLO.bit_length() - 1, None,
                                  ALU.logical_shift_right).then_inc(bucket_step, 1)
                dve.tensor_scalar(digits_i[:, 1, :], buckets_i, BLO - 1, None, ALU.bitwise_and).then_inc(bucket_step, 1)
                dve.wait_ge(bucket_step, 4)
                dve.wait_ge(iota_floated, 2)

                def hot(m, a):
                    turn = m * 2 + a
                    wait_later(dve, counted, turn - 1)
                    for d, at, width in ((0, 0, BHI), (1, BHI, BLO)):
                        last = dve.tensor_tensor(
                            digit_hot[:, a, :, at:at + width],
                            iota[:, 0:width].unsqueeze(1).broadcast_to([P, COUNT, width]),
                            digits_i[:, d, ds(turn * COUNT, COUNT)].unsqueeze(2).broadcast_to([P, COUNT, width]),
                            ALU.is_equal)
                    last.then_inc(digits_hot, 1)
                hot(0, 0)
                hot(0, 1)
                with dve.Fori(1, count_turns // 2) as m:
                    hot(m, 0)
                    hot(m, 1)
                dve.wait_ge(counted, count_turns)
                dve.tensor_copy(counts[:, :], bank[6][0:BHI, 0:BLO]).then_inc(counts_out, 1)
                dve.wait_ge(vec_turned, 1)
                dve.tensor_copy(vecT[:, :], bank[7][:, 0:NV]).then_inc(vec_turned, 1)
                dve.wait_ge(counts_back, 16)
                dve.wait_ge(consts_set, 4)
                dve.tensor_tensor_scan(count_row[:, 1, :], zeros[0:1, :, :].rearrange("p k n -> p (k n)")[:, 0:NBK],
                                       count_row[:, 0, :], 0.0, ALU.add, ALU.add).then_inc(count_step, 1)
                dve.wait_ge(count_step, 1)
                dve.tensor_tensor(count_row[:, 2, :], count_row[:, 1, :], count_row[:, 0, :], ALU.subtract)\
                    .then_inc(count_step, 1)

        nc.all_engine_barrier()

        x_in, rows0_out, y0_out = sem("x_in"), sem("rows0_out"), sem("y0_out")
        stats_made, mv_made, sd_made, rstd_made = sem("stats_made"), sem("mv_made"), sem("sd_made"), sem("rstd_made")
        rows_made, turned0, turned0_out, projected0, y0_made = (sem("rows_made"), sem("turned0"), sem("turned0_out"),
                                                                sem("projected0"), sem("y0_made"))
        buckets_hot, ranked, rank_read, rank_cut, rows_known = (
            sem("buckets_hot"), sem("ranked"), sem("rank_read"), sem("rank_cut"), sem("rows_known"))
        record_made, rank_whole = sem("record_made"), sem("rank_whole")
        scattered = [sem(f"scattered{i}") for i in range(2)]

        BT = 4
        sort_turns = -(-chunks // SORT)
        assert BT * NB <= chunks // SORT

        def sort_loop(engine, turn, node_work=None):
            def block_turns(b):
                for j in range(BT):
                    turn(b * (BT // 2) + j // 2, j % 2, b * BT + j)
                    if node_work:
                        node_work(b, j)
            block_turns(0)
            with engine.Fori(1, NB) as b:
                block_turns(b)
            for n in range(BT * NB, sort_turns):
                turn(n // 2, n % 2, n)

        def in_turn(n):
            return min(SORT, chunks - n * SORT) if isinstance(n, int) else SORT

        with nc.Block() as block:
            @block.vector
            def _(dve):
                def turn(m, a, n):
                    k = in_turn(n)
                    wait_later(dve, ranked, (n - 1) * SORT)
                    dve.tensor_tensor(bucket_hot[:, a, 0:k, :], iota_b[:, :].unsqueeze(1).broadcast_to([P, k, NBK]),
                                      buckets[:, ds(n * SORT, k)].unsqueeze(2).broadcast_to([P, k, NBK]),
                                      ALU.is_equal).then_inc(buckets_hot, 1)
                    dve.wait_ge(buckets_hot, n + 1)
                    for c in range(k):
                        dve.wait_ge(ranked, n * SORT + c + 1)
                        wait_later(dve, rank_read, n * SORT + c - 1)
                        dve.tensor_tensor_reduce(hot_rank[:, c % 2, :], bank[(a * SORT + c) % 2][:, 0:NBK],
                                                 bucket_hot[:, a, c, :],
                                                 1.0, 0.0, ALU.mult, ALU.add, rank_f[:, a, c:c + 1]).then_inc(rank_read, 1)
                    dve.wait_ge(rank_read, n * SORT + k)
                    dve.tensor_copy(rank_i[:, 0, a, 0:k], rank_f[:, a, 0:k]).then_inc(rank_whole, 1)
                    dve.wait_ge(rank_whole, n + 1)
                    dve.tensor_scalar(rank_i[:, 1, a, 0:k], rank_i[:, 0, a, 0:k], P - 1, None, ALU.bitwise_and)
                    dve.tensor_scalar(rank_i[:, 2, a, 0:k], rank_i[:, 0, a, 0:k], P.bit_length() - 1, None,
                                      ALU.logical_shift_right).then_inc(rank_cut, 1)
                    dve.wait_ge(rank_cut, n + 1)
                    wait_later(dve, scattered[a], 16 * SORT * m)
                    dve.scalar_tensor_tensor(out=row_idx[:, a, 0:k], in0=rank_i[:, 1, a, 0:k], scalar=float(chunks),
                                             in1=rank_i[:, 2, a, 0:k], op0=ALU.mult, op1=ALU.add).then_inc(rows_known, 1)

                def node_work(b, j):
                    if j == 0:
                        dve.wait_ge(x_in, b * 16 + 16)
                        dve.bn_stats(stats[0:B, 0, :], x_blk).then_inc(stats_made, 1)
                        dve.wait_ge(stats_made, b + 1)
                        dve.nop(nofuse=True)
                        dve.bn_aggr(mv[0:B, 0, :], stats[0:B, 0, :]).then_inc(mv_made, 1)
                        dve.wait_ge(sd_made, b + 1)
                        dve.reciprocal(rstd[0:B, 0:1], sd[0:B, 0:1]).then_inc(rstd_made, 1)
                        dve.wait_ge(rstd_made, b + 1)
                        wait_later(dve, rows0_out, b * 16)
                        wait_later(dve, turned0, b)
                        dve.tensor_scalar(row_blk, x_blk, mv[0:B, 0, 0:1], rstd[0:B, 0:1], ALU.subtract, ALU.mult)\
                            .then_inc(rows_made, 1)
                    if j == BT - 1:
                        dve.wait_ge(projected0, b + 1)
                        wait_later(dve, y0_out, b * 16)
                        dve.tensor_tensor(y_blk, bank[3][0:B, 0:D], x_blk, ALU.add).then_inc(y0_made, 1)
                sort_loop(dve, turn, node_work)

            @block.tensor
            def _(pe):
                pe.wait_ge(count_step, 2)
                for q in range(2):
                    pe.matmul(bank[q][:, 0:NBK], ones[0:1, :], count_row[0:1, 2, :], start=True, stop=True,
                              skip_group_check=True)

                def add(q, which, hot):
                    return pe.matmul(bank[q][:, 0:NBK], which[:, :], hot, start=False, stop=True, skip_group_check=True)

                def turn(m, a, n):
                    k = in_turn(n)
                    pe.wait_ge(buckets_hot, n + 1)
                    for c in range(k):
                        q = (a * SORT + c) % 2
                        hot = bucket_hot[:, a, c, :]
                        add(q, before, hot).then_inc(ranked, 1)
                        if c or not isinstance(n, int) or n:
                            prev = bucket_hot[:, a, c - 1, :] if c else bucket_hot[:, 1 - a, SORT - 1, :]
                            pe.wait_ge(rank_read, n * SORT + c)
                            add(1 - q, not_before, prev)
                        add(1 - q, all_ones, hot)

                def node_work(b, j):
                    if j == 1:
                        pe.wait_ge(rows_made, b + 1)
                        wait_later(pe, turned0_out, b)
                        for k in range(DK):
                            last = pe.transpose(bank[2][:, k * B:(k + 1) * B], row_blk[:, k * P:(k + 1) * P],
                                                ident[0:B, 0:B])
                        last.then_inc(turned0, 1)
                    if j == 2:
                        pe.wait_ge(turned0_out, b + 1)
                        wait_later(pe, y0_made, b)
                        for k in range(DK):
                            pe.matmul(bank[3][0:B, 0:D], colT[:, 0, k, :], Wg[:, k, :], start=(k == 0), stop=False)
                        pe.matmul(bank[3][0:B, 0:D], ones[0:1, 0:B], bg[:, :], start=False, stop=True)\
                            .then_inc(projected0, 1)
                sort_loop(pe, turn, node_work)

            @block.scalar
            def _(act):
                act.wait_ge(loaded[1], 32)
                act.wait_ge(loaded[2], 32)

                def turn(m, a, n):
                    k = in_turn(n)
                    wait_later(act, scattered[a], 16 * SORT * m)
                    cols = ds(n * SORT, k)
                    act.activation(record[:, a, 0:k, 0], raw_i[:, 1, cols], ACT.Copy)
                    act.activation(record[:, a, 0:k, 1], raw[:, 2, cols], ACT.Copy)
                    act.activation(record[:, a, 0:k, 2], raw_i[:, 0, cols], ACT.Copy)
                    act.activation(record[:, a, 0:k, 3], raw[:, 2, cols], ACT.Copy).then_inc(record_made, 1)

                def node_work(b, j):
                    if j == 0:
                        act.wait_ge(mv_made, b + 1)
                        act.activation(sd[0:B, 0:1], mv[0:B, 0, 1:2], ACT.Sqrt, bias=eps[0:B, :]).then_inc(sd_made, 1)
                    if j == 1:
                        act.wait_ge(turned0, b + 1)
                        wait_later(act, projected0, b)
                        act.activation(colT[:, 0].rearrange("p k n -> p (k n)"), bank[2][:, 0:DK * B],
                                       ACT.Copy).then_inc(turned0_out, 1)
                sort_loop(act, turn, node_work)

            @block.gpsimd
            def _(pool):
                def turn(m, a, n):
                    k = in_turn(n)
                    pool.wait_ge(record_made, n + 1)
                    pool.nop(nofuse=True)
                    pool.wait_ge(rows_known, n + 1)
                    pool.nop(nofuse=True)
                    for c in range(k):
                        pool.indirect_dma_start(
                            out=sorted_edges, out_offset=bass.IndirectOffsetOnAxis(ap=row_idx[:, a, c:c + 1], axis=0),
                            in_=record[:, a, c, :], in_offset=None).then_inc(scattered[a], 16)
                sort_loop(pool, turn)

            @block.sync
            def _(sp):
                def rows(arr, b):
                    return arr[ds(b * B, B), :]

                def node_work(b):
                    wait_later(sp, y0_made, b)
                    sp.dma_start(x_blk, rows(x, b)).then_inc(x_in, 16)
                    sp.wait_ge(rows_made, b + 1)
                    sp.dma_start(rows(xn0_rows, b), row_blk).then_inc(rows0_out, 16)
                    sp.wait_ge(y0_made, b + 1)
                    sp.dma_start(rows(y_rows, b), y_blk).then_inc(y0_out, 16)
                node_work(0)
                with sp.Fori(1, NB) as b:
                    node_work(b)
                sp.wait_ge(rows0_out, 16 * NB)
                sp.wait_ge(y0_out, 16 * NB)
                for a in range(2):
                    n_chunks = sum(in_turn(n) for n in range(sort_turns) if n % 2 == a)
                    sp.wait_ge(scattered[a], 16 * n_chunks)

        nc.all_engine_barrier()

        back_loaded, table_pads, tables_out, ext_made, ext_turned, ext_grouped = (
            sem("back_loaded"), sem("table_pads"), sem("tables_out"), sem("ext_made"), sem("ext_turned"), sem("ext_grouped"))
        win_stored, win_back, win_float, span_step, due_step = (sem("win_stored"), sem("win_back"), sem("win_float"),
                                                                sem("span_step"), sem("due_step"))
        with nc.Block() as block:
            @block.sync
            def _(sp):
                sp.dma_start(back.rearrange("p c r -> p (c r)"), sorted_edges.rearrange("(p c) r -> p (c r)", p=P))\
                    .then_inc(back_loaded, 16)
                sp.wait_ge(ext_grouped, 2)
                for t in range(2):
                    sp.dma_start(window_dram[t, :].rearrange("(q k) -> q k", q=P), group_ext[:, t, :])\
                        .then_inc(win_stored, 16)
                sp.wait_ge(win_stored, 32)
                sp.dma_start(window[:, :, :], window_dram.partition_broadcast(P)).then_inc(win_back, 16)

            @block.gpsimd
            def _(pool):
                if used > chunks:
                    pool.memset(gatherT[:, chunks:used], 0.0).then_inc(table_pads, 1)
                    pool.memset(wT[:, chunks:used], 0.0).then_inc(table_pads, 1)
                    pool.memset(relT[:, chunks:used], float(N - 1)).then_inc(table_pads, 1)
                pool.memset(ext_part[:, :, groups:group_cols], 0.0).then_inc(table_pads, 1)
                pool.wait_ge(tables_out, 3)
                pool.memset(accT[:, :, :], 0.0)

            @block.scalar
            def _(act):
                act.wait_ge(back_loaded, 16)
                act.activation(gatherT[:, 0:chunks], back[:, :, 0], ACT.Copy).then_inc(tables_out, 1)
                act.activation(wT[:, 0:chunks], back[:, :, 1], ACT.Copy).then_inc(tables_out, 1)

            @block.tensor
            def _(pe):
                pe.wait_ge(ext_made, 2)
                for t in range(2):
                    for k in range(group_sets):
                        last = pe.transpose(bank[2 + t][:, k * P:(k + 1) * P],
                                            ext_part[:, t, :].rearrange("p (q k) -> p k q", q=P)[:, k, :], ident[:, :])
                last.then_inc(ext_turned, 1)

            @block.vector
            def _(dve):
                dve.wait_ge(back_loaded, 16)
                dve.tensor_copy(relT[:, 0:chunks], back[:, :, 2]).then_inc(tables_out, 1)
                dve.wait_ge(tables_out, 3)
                dve.wait_ge(table_pads, 1 + 3 * (used > chunks))
                rel = relT[:, :].rearrange("p (g c) -> p g c", c=CG)
                dve.tensor_reduce(ext_part[:, 0, 0:groups], rel, AX, ALU.min).then_inc(ext_made, 1)
                dve.tensor_reduce(ext_part[:, 1, 0:groups], rel, AX, ALU.max).then_inc(ext_made, 1)
                dve.wait_ge(ext_turned, 1)
                for t, op in ((0, ALU.min), (1, ALU.max)):
                    dve.tensor_reduce(group_ext[:, t, :], bank[2 + t][:, 0:group_cols].rearrange("q (k p) -> q k p", p=P),
                                      AX, op).then_inc(ext_grouped, 1)
                dve.wait_ge(win_back, 16)
                dve.tensor_copy(windowf[:, :, :], window[:, :, :]).then_inc(win_float, 1)
                dve.tensor_copy(base_i[:, :], window[:, 0, :]).then_inc(win_float, 1)
                dve.wait_ge(win_float, 2)
                dve.tensor_tensor(rel, rel, windowf[:, 0, 0:groups].unsqueeze(2).broadcast_to([P, groups, CG]),
                                  ALU.subtract).then_inc(win_float, 1)
                dve.tensor_tensor(windowf[:, 1, :], windowf[:, 1, :], windowf[:, 0, :], ALU.subtract).then_inc(span_step, 1)
                dve.wait_ge(span_step, 1)
                dve.tensor_reduce(span[:, 0:1], windowf[:, 1, 0:groups], AX, ALU.max).then_inc(span_step, 1)
                dve.wait_ge(span_step, 2)
                dve.tensor_copy(rounds_all[:, 0:1], span[:, 0:1]).then_inc(span_step, 1)
                dve.wait_ge(span_step, 3)
                dve.tensor_scalar(rounds_i[0:1, 1:2], rounds_all[0:1, 0:1], WIN.bit_length() - 1, None,
                                  ALU.logical_shift_right)
                dve.tensor_scalar(due_i[0:1, 0:groups], iota_i[0:1, 0:groups], BG - LEAD * GPI + SLACK, 0,
                                  ALU.add, ALU.max).then_inc(due_step, 1)
                dve.wait_ge(due_step, 1)
                dve.tensor_scalar(due_i[0:1, 0:groups], due_i[0:1, 0:groups], BG.bit_length() - 1, None,
                                  ALU.logical_shift_right).then_inc(due_step, 1)
                dve.wait_ge(due_step, 2)
                dve.tensor_scalar(due[0:1, 0:groups], due_i[0:1, 0:groups], float(B), None, ALU.mult).then_inc(due_step, 1)
                dve.wait_ge(due_step, 3)
                dve.tensor_tensor(due[0:1, 0:groups], due[0:1, 0:groups], windowf[0:1, 0, 0:groups], ALU.subtract)\
                    .then_inc(due_step, 1)
                dve.wait_ge(due_step, 4)
                dve.tensor_reduce(span[0:1, 3:4], due[0:1, 0:groups], AX, ALU.max).then_inc(due_step, 1)
                dve.wait_ge(due_step, 5)
                dve.tensor_scalar(span[0:1, 2:3], span[0:1, 0:1], float(1 - WIN), None, ALU.add).then_inc(due_step, 1)
                dve.wait_ge(due_step, 6)
                dve.tensor_tensor(span[0:1, 1:2], span[0:1, 2:3], span[0:1, 3:4], ALU.max).then_inc(due_step, 1)
                dve.wait_ge(due_step, 7)
                dve.tensor_scalar(rounds_i[0:1, 0:1], span[0:1, 1:2], 0.0, None, ALU.max)
                dve.tensor_scalar(rounds_all[:, 1:2], rounds_all[:, 0:1], -WIN, None, ALU.bitwise_and).then_inc(span_step, 1)

        nc.all_engine_barrier()
        more_rounds = nc.values_load(rounds_i[0:1, 1:2], min_val=0, max_val=(N - 1) // WIN)
        too_late = nc.values_load(rounds_i[0:1, 0:1], min_val=0, max_val=N + NB * B)

        landed = [sem(f"landed{i}") for i in range(RING)]
        ring_free = sem("ring_free")
        idx_ready, compared, onehot_ready, psum_free = (
            sem("idx_ready"), sem("compared"), sem("onehot_ready"), sem("psum_free"))
        hop_sems = range(ring_free.num, psum_free.num + 1)
        landed_sems = range(landed[0].num, landed[-1].num + 1)

        def all_turns(engine, turn):
            turn(0)
            with engine.Fori(1, turns - 1) as i:
                turn(i)
            turn(turns - 1)

        edge_bank = bank[6:8]

        def stage_indices(act, i, h):
            wait_later(act, ring_free, (i - 1) * RING + CG * (h + 1))
            act.activation(idx_stage[:, h, :], gatherT[:, ds(i * RING + h * CG, CG)], ACT.Copy).then_inc(idx_ready, 1)

        def gather_group(pool, rows, i, h):
            pool.wait_ge(idx_ready, i * GPI + h + 1)
            pool.nop(nofuse=True)
            for c in range(CG):
                s = h * CG + c
                pool.indirect_dma_start(
                    out=ring[:, s, :], out_offset=None, in_=rows,
                    in_offset=bass.IndirectOffsetOnAxis(ap=idx_stage[:, h, c:c + 1], axis=0),
                ).then_inc(landed[s], 16)

        def weigh(dve, i, h):
            g = i * GPI + h
            cols = ds(i * RING + h * CG, CG)
            dve.tensor_tensor(onehot[:, h], iota[:, 0:WIN].unsqueeze(1).broadcast_to([P, CG, WIN]),
                              relT[:, cols].unsqueeze(2).broadcast_to([P, CG, WIN]), ALU.is_equal)\
                .then_inc(compared, 1)
            dve.wait_ge(compared, g + 1)
            dve.tensor_tensor(onehot[:, h], onehot[:, h], wT[:, cols].unsqueeze(2).broadcast_to([P, CG, WIN]),
                              ALU.mult).then_inc(onehot_ready, 1)

        def weigh_next(dve, i, h):
            if h + 1 < GPI:
                weigh(dve, i, h + 1)
            elif not isinstance(i, int) or i + 1 < turns:
                weigh(dve, i + 1, 0)

        def add_group(dve, i, h):
            g = i * GPI + h
            base = dve.value_load(base_i[0:1, ds(g, 1)], min_val=0, max_val=N)
            dve.wait_ge(ring_free, CG * (g + 1))
            wait_later(dve, psum_free, g)
            to = accT[:, :, ds(base, WIN)]
            dve.tensor_tensor(to, to, edge_bank[h][:, 0:DK * WIN].rearrange("p (k w) -> p k w", k=DK), ALU.add)\
                .then_inc(psum_free, 1)

        def edge_products(pe, passes, i, h):
            g = i * GPI + h
            wait_later(pe, psum_free, g - 1)
            pe.wait_ge(onehot_ready, g + 1)
            for c in range(CG):
                s = h * CG + c
                pe.wait_ge(landed[s], (passes * turns + i) * 16 + 16)
                for k in range(DK):
                    last = pe.matmul(edge_bank[h][:, k * WIN:(k + 1) * WIN], ring[:, s, k * P:(k + 1) * P],
                                     onehot[:, h, c, :], start=(c == 0 and k == 0),
                                     stop=(c == CG - 1), skip_group_check=True)
                last.then_inc(ring_free, 1)

        def edge_pass(rows):
            with nc.Block() as block:
                @block.scalar
                def _(act):
                    def turn(i):
                        for h in range(GPI):
                            stage_indices(act, i, h)
                    all_turns(act, turn)

                @block.gpsimd
                def _(pool):
                    def turn(i):
                        for h in range(GPI):
                            gather_group(pool, rows, i, h)
                    all_turns(pool, turn)

                @block.vector
                def _(dve):
                    def turn(i):
                        for h in range(GPI):
                            weigh_next(dve, i, h)
                            add_group(dve, i, h)
                    weigh(dve, 0, 0)
                    all_turns(dve, turn)

                @block.tensor
                def _(pe):
                    def turn(i):
                        for h in range(GPI):
                            edge_products(pe, 0, i, h)
                    all_turns(pe, turn)
            nc.all_engine_barrier(sems_to_clear=hop_sems)
            nc.gpsimd.dma_reset(landed_sems)
            nc.all_engine_barrier(sems_to_clear=landed_sems)

        shifted = sem("shifted")

        def shift_windows(restore):
            with nc.Block() as block:
                @block.vector
                def _(dve):
                    if restore:
                        dve.tensor_copy(span[:, 2:3], rounds_all[:, 1:2]).then_inc(shifted, 1)
                        dve.wait_ge(shifted, 1)
                        dve.tensor_scalar(relT[:, 0:used], relT[:, 0:used], span[:, 2:3], float(WIN), ALU.add, ALU.add)
                        dve.tensor_copy(base_i[:, :], windowf[:, 0, :])
                    else:
                        dve.tensor_scalar(relT[:, 0:used], relT[:, 0:used], -float(WIN), None, ALU.add)
                        dve.tensor_scalar(base_i[:, :], base_i[:, :], float(WIN), float(N), ALU.add, ALU.min)
            nc.all_engine_barrier(sems_to_clear=range(shifted.num, shifted.num + 1))

        def with_edges(edges, b):
            return edges and (not isinstance(b, int) or b < edge_steps)

        def turn_beside(b, q):
            return b * 2 + LEAD + q // GPI, q % GPI

        def next_indices(act, edges, b, q):
            i, h = turn_beside(b, q)
            if with_edges(edges, b) and (not isinstance(i, int) or i + 1 < turns):
                stage_indices(act, i + 1, h)

        def wait_for_block(act, edges, b):
            if edges:
                done = b * BG + LEAD * GPI - SLACK
                act.wait_ge(psum_free, min(done, groups) if isinstance(b, int) else done)

        y1_in, y1_out, rows1_out = sem("y1_in"), sem("y1_out"), sem("rows1_out")
        cols_copied, turned1, rows1_made, projected1, y1_made = (
            sem("cols_copied"), sem("turned1"), sem("rows1_made"), sem("projected1"), sem("y1_made"))
        mid_sems = range(y1_in.num, y1_made.num + 1)

        def rows_pass(edges):
            def run(engine, step, lead=None):
                if edges and lead:
                    lead(0)
                    with engine.Fori(1, LEAD) as i:
                        lead(i)
                step(0)
                if edges:
                    with engine.Fori(1, edge_steps - 1) as b:
                        step(b)
                    for b in range(edge_steps - 1, NB):
                        step(b)
                else:
                    with engine.Fori(1, NB) as b:
                        step(b)

            with nc.Block() as block:
                @block.sync
                def _(sp):
                    def step(b):
                        wait_later(sp, y1_out, b * 16)
                        sp.dma_start(y_blk, y_rows[ds(b * B, B), :]).then_inc(y1_in, 16)
                        sp.wait_ge(rows1_made, b + 1)
                        sp.dma_start(hop1_rows[ds(b * B, B), :], row_blk).then_inc(rows1_out, 16)
                        sp.wait_ge(y1_made, b + 1)
                        sp.dma_start(y_rows[ds(b * B, B), :], y_blk).then_inc(y1_out, 16)
                    run(sp, step)
                    sp.wait_ge(rows1_out, 16 * NB)
                    sp.wait_ge(y1_out, 16 * NB)

                if edges:
                    @block.gpsimd
                    def _(pool):
                        def turn(i):
                            for h in range(GPI):
                                gather_group(pool, xn0_rows, i, h)
                        all_turns(pool, turn)

                @block.scalar
                def _(act):
                    def lead(i):
                        for h in range(GPI):
                            stage_indices(act, i + 1, h)

                    def step(b):
                        wait_for_block(act, edges, b)
                        wait_later(act, projected1, b)
                        cols = accT[:, :, ds(b * B, B)]
                        act.activation(colT[:, 0], cols, ACT.Copy).then_inc(cols_copied, 1)
                        act.wait_ge(cols_copied, b + 1)
                        act.nop(nofuse=True)
                        act.activation(cols, zeros[:, :, :], ACT.Copy)
                        for q in range(2):
                            next_indices(act, edges, b, q)
                        act.wait_ge(turned1, b + 1)
                        wait_later(act, rows1_out, b * 16)
                        act.activation(row_blk, bank[2][0:B, 0:D], ACT.Copy).then_inc(rows1_made, 1)
                        for q in range(2, BG):
                            next_indices(act, edges, b, q)
                    if edges:
                        for h in range(GPI):
                            stage_indices(act, 0, h)
                    run(act, step, lead)

                @block.vector
                def _(dve):
                    def edge_group(i, h):
                        weigh_next(dve, i, h)
                        add_group(dve, i, h)

                    def lead(i):
                        for h in range(GPI):
                            edge_group(i, h)

                    def step(b):
                        for q in range(3):
                            if with_edges(edges, b):
                                edge_group(*turn_beside(b, q))
                        dve.wait_ge(y1_in, b * 16 + 16)
                        dve.wait_ge(projected1, b + 1)
                        dve.tensor_tensor(y_blk, bank[3][0:B, 0:D], y_blk, ALU.add).then_inc(y1_made, 1)
                        if with_edges(edges, b):
                            edge_group(*turn_beside(b, 3))
                    if edges:
                        weigh(dve, 0, 0)
                    run(dve, step, lead)

                @block.tensor
                def _(pe):
                    def lead(i):
                        for h in range(GPI):
                            edge_products(pe, 0, i, h)

                    def step(b):
                        def edge_group(q):
                            if with_edges(edges, b):
                                edge_products(pe, 0, *turn_beside(b, q))
                        edge_group(0)
                        pe.wait_ge(cols_copied, b + 1)
                        wait_later(pe, rows1_made, b)
                        for k in range(DK):
                            last = pe.transpose(bank[2][0:B, k * P:(k + 1) * P], colT[:, 0, k, :], ident[:, :])
                        last.then_inc(turned1, 1)
                        edge_group(1)
                        wait_later(pe, y1_made, b)
                        for k in range(DK):
                            last = pe.matmul(bank[3][0:B, 0:D], colT[:, 0, k, :], Wg[:, DK + k, :],
                                             start=(k == 0), stop=(k == DK - 1))
                        last.then_inc(projected1, 1)
                        edge_group(2)
                        edge_group(3)
                    run(pe, step, lead)
            nc.all_engine_barrier(sems_to_clear=mid_sems)

        y_here = [sem(f"y_here{i}") for i in range(2)]
        hop_copied, gnn_done, x1_made = sem("hop_copied"), sem("gnn_done"), sem("x1_made")
        stats1_made, mv1_made, sd1_made, rstd1_made, z1_made = (
            sem("stats1_made"), sem("mv1_made"), sem("sd1_made"), sem("rstd1_made"), sem("z1_made"))
        stats2_made, mv2_made, sd2_made, rstd2_made, z2_made = (
            sem("stats2_made"), sem("mv2_made"), sem("sd2_made"), sem("rstd2_made"), sem("z2_made"))
        z_turned, xn_ready, scored = sem("z_turned"), sem("xn_ready"), sem("scored")
        logits_out, top_made, idx_made, idxf_made, gap_made, tanh_made = (
            sem("logits_out"), sem("top_made"), sem("idx_made"), sem("idxf_made"), sem("gap_made"), sem("tanh_made"))
        share_made, pick_made, gates_made, gates_turned, gatesT_out, bias_mixed = (
            sem("share_made"), sem("pick_made"), sem("gates_made"), sem("gates_turned"), sem("gatesT_out"),
            sem("bias_mixed"))
        acc_made, hidden_made, gelu_made, expert_done = (
            sem("acc_made"), sem("hidden_made"), sem("gelu_made"), sem("expert_done"))
        stored = [sem(f"stored{i}") for i in range(2)]

        psH, psY = bank[0:2], bank[2:4]
        psG, psS = bank[4], bank[5]
        SCORE, GATE = 2 * P, 3 * P
        ACCS = NX + 1

        def dense(edges):
            def run(engine, step, lead=None):
                if edges and lead:
                    lead(0)
                    with engine.Fori(1, LEAD) as i:
                        lead(i)
                step(0, 0, True, False)
                step(1, 1, True, True)
                step(2, 0, True, True)
                pairs = (edge_steps - 3) // 2 if edges else NB // 2 - 1
                with engine.Fori(1, pairs) as m:
                    step(m * 2 + 1, 1, True, True)
                    step(m * 2 + 2, 0, True, True)
                for b in range(2 * pairs + 1, NB):
                    step(b, b % 2, True, True)
                step(NB, 0, False, True)

            with nc.Block() as block:
                @block.sync
                def _(sp):
                    def step(b, a, front, back):
                        if front:
                            wait_later(sp, x1_made, b)
                            sp.dma_start(y_in[0:B, a, :], y_rows[ds(b * B, B), :]).then_inc(y_here[a], 16)
                        if back:
                            sp.wait_ge(acc_made, ACCS * b)
                            sp.dma_start(out[ds((b - 1) * B, B), :], acc[0:B, 1 - a, :]).then_inc(stored[1 - a], 16)
                    run(sp, step)
                    for a in range(2):
                        sp.wait_ge(stored[a], 16 * (NB // 2))

                if edges:
                    @block.gpsimd
                    def _(pool):
                        def turn(i):
                            for h in range(GPI):
                                gather_group(pool, hop1_rows, i, h)
                        all_turns(pool, turn)

                @block.tensor
                def _(pe):
                    pe.wait_ge(weights_loaded, 32)

                    def lead(i):
                        for h in range(GPI):
                            edge_products(pe, 1, i, h)

                    def step(b, a, front, back):
                        o = 1 - a
                        e0 = (b - 1) * NX

                        def edge_group(q):
                            if with_edges(edges, b):
                                edge_products(pe, 1, *turn_beside(b, q))

                        def hidden(e):
                            wait_later(pe, gelu_made, e0 + max(e - 1, 0))
                            for c in range(HC):
                                for k in range(DK):
                                    last = pe.matmul(psH[e % 2][:, c * B:(c + 1) * B], W1s[:, e, k, c * P:(c + 1) * P],
                                                     xnT[:, o, k, :], start=(k == 0), stop=(k == DK - 1))
                            last.then_inc(hidden_made, 1)

                        def expert_out(e):
                            pe.wait_ge(gelu_made, e0 + e + 1)
                            wait_later(pe, acc_made, ACCS * (b - 1) + e)
                            for c in range(HC):
                                last = pe.matmul(psY[e % 2][0:B, 0:D], gelu_out[:, e % 2, c, :], W2s[:, e, c, :],
                                                 start=(c == 0), stop=(c == HC - 1))
                            last.then_inc(expert_done, 1)

                        def gnn_term():
                            pe.wait_ge(hop_copied, b + 1)
                            wait_later(pe, acc_made, ACCS * (b - 1) + 1)
                            for k in range(DK):
                                last = pe.matmul(psG[0:B, 0:D], hopT[:, a, k, :], Wg[:, 2 * DK + k, :],
                                                 start=(k == 0), stop=(k == DK - 1))
                            last.then_inc(gnn_done, 1)

                        def turn_rows():
                            pe.wait_ge(z2_made, b + 1)
                            for k in range(DK):
                                last = pe.transpose(psS[:, k * B:(k + 1) * B], z[0:B, a, k * P:(k + 1) * P],
                                                    ident[0:B, 0:B])
                            last.then_inc(z_turned, 1)

                        def scores():
                            pe.wait_ge(xn_ready, b + 1)
                            for k in range(DK):
                                last = pe.matmul(psS[0:B, SCORE:SCORE + NX], xnT[:, a, k, :], Wrs[:, k, :],
                                                 start=(k == 0), stop=(k == DK - 1))
                            last.then_inc(scored, 1)

                        def turn_gates():
                            pe.wait_ge(gates_made, b + 1)
                            pe.transpose(psS[0:NX, GATE:GATE + B], w_full[0:B, a, :], ident[0:B, 0:B])\
                                .then_inc(gates_turned, 1)

                        def mix_bias():
                            pe.wait_ge(gatesT_out, b + 1)
                            pe.matmul(psG[0:B, 0:D], wfT[:, :], b2s[:, :], start=True, stop=True).then_inc(bias_mixed, 1)

                        if back:
                            hidden(0)
                        if front:
                            gnn_term()
                        if back:
                            for e in range(NX):
                                if e + 1 < NX:
                                    hidden(e + 1)
                                if e % 2 == 0:
                                    edge_group(e // 2)
                                expert_out(e)
                                if front:
                                    if e == 3:
                                        turn_rows()
                                    if e == 4:
                                        scores()
                                    if e == 6:
                                        turn_gates()
                                    if e == 7:
                                        mix_bias()
                        elif front:
                            for q in range(BG):
                                edge_group(q)
                            turn_rows()
                            scores()
                            turn_gates()
                            mix_bias()
                    run(pe, step, lead)

                @block.scalar
                def _(act):
                    def lead(i):
                        for h in range(GPI):
                            stage_indices(act, i + 1, h)

                    def step(b, a, front, back):
                        e0 = (b - 1) * NX

                        def gelu(e):
                            act.wait_ge(hidden_made, e0 + e + 1)
                            wait_later(act, expert_done, e0 + max(e - 1, 0))
                            for c in range(HC):
                                last = act.activation(gelu_out[:, e % 2, c, :], psH[e % 2][:, c * B:(c + 1) * B],
                                                      ACT.Gelu, bias=vecT[:, e * HC + c:e * HC + c + 1])
                            last.then_inc(gelu_made, 1)

                        if front:
                            wait_for_block(act, edges, b)
                            wait_later(act, gnn_done, b)
                            act.activation(hopT[:, a], accT[:, :, ds(b * B, B)], ACT.Copy).then_inc(hop_copied, 1)
                        if back:
                            gelu(0)
                        if front:
                            act.wait_ge(mv1_made, b + 1)
                            act.activation(sd[0:B, 0:1], mv[0:B, 0, 1:2], ACT.Sqrt, bias=eps[0:B, :]).then_inc(sd1_made, 1)
                            act.wait_ge(mv2_made, b + 1)
                            act.activation(sd[0:B, 1:2], mv[0:B, 1, 1:2], ACT.Sqrt, bias=eps[0:B, :]).then_inc(sd2_made, 1)
                        if back:
                            gelu(1)
                            next_indices(act, edges, b, 0)
                            gelu(2)
                            gelu(3)
                            next_indices(act, edges, b, 1)
                            gelu(4)
                        elif front:
                            for q in range(BG):
                                next_indices(act, edges, b, q)
                        if front:
                            act.wait_ge(z_turned, b + 1)
                            for k in range(DK):
                                g = NX * HC + k
                                last = act.activation(xnT[:, a, k, :], psS[:, k * B:(k + 1) * B], ACT.Identity,
                                                      scale=vecT[:, g:g + 1], bias=vecT[:, g + DK:g + DK + 1])
                            last.then_inc(xn_ready, 1)
                        if back:
                            gelu(5)
                            next_indices(act, edges, b, 2)
                        if front:
                            act.wait_ge(gap_made, b + 1)
                            act.activation(pair[0:B, 1:2], pair[0:B, 0:1], ACT.Tanh, scale=0.5).then_inc(tanh_made, 1)
                        if back:
                            gelu(6)
                            gelu(7)
                            next_indices(act, edges, b, 3)
                    if edges:
                        for h in range(GPI):
                            stage_indices(act, 0, h)
                    run(act, step, lead)

                @block.vector
                def _(dve):
                    def lead(i):
                        for h in range(GPI):
                            weigh_next(dve, i, h)
                            add_group(dve, i, h)

                    def step(b, a, front, back):
                        o = 1 - a
                        e0 = (b - 1) * NX

                        def edge_group(q):
                            if with_edges(edges, b):
                                i, h = turn_beside(b, q)
                                weigh_next(dve, i, h)
                                add_group(dve, i, h)

                        def add_expert(e):
                            dve.wait_ge(expert_done, e0 + e + 1)
                            dve.wait_ge(acc_made, ACCS * (b - 1) + e + 1)
                            dve.scalar_tensor_tensor(out=acc[0:B, o, :], in0=psY[e % 2][0:B, 0:D],
                                                     scalar=w_full[0:B, o, e:e + 1], in1=acc[0:B, o, :],
                                                     op0=ALU.mult, op1=ALU.add).then_inc(acc_made, 1)

                        def norm_stats(src_tile, n, made_st, made_mv):
                            dve.bn_stats(stats[0:B, n, :], src_tile).then_inc(made_st, 1)
                            dve.wait_ge(made_st, b + 1)
                            dve.nop(nofuse=True)
                            dve.bn_aggr(mv[0:B, n, :], stats[0:B, n, :]).then_inc(made_mv, 1)

                        def normalize(dst_tile, src_tile, n, made_sd, made_rs, made_z):
                            dve.wait_ge(made_sd, b + 1)
                            dve.reciprocal(rstd[0:B, n:n + 1], sd[0:B, n:n + 1]).then_inc(made_rs, 1)
                            dve.wait_ge(made_rs, b + 1)
                            dve.tensor_scalar(dst_tile, src_tile, mv[0:B, n, 0:1], rstd[0:B, n:n + 1],
                                              ALU.subtract, ALU.mult).then_inc(made_z, 1)
                            dve.wait_ge(made_z, b + 1)

                        def two_norms():
                            dve.wait_ge(gnn_done, b + 1)
                            dve.wait_ge(y_here[a], (b - a) * 8 + 16)
                            dve.tensor_tensor(x1[0:B, a, :], psG[0:B, 0:D], y_in[0:B, a, :], ALU.add).then_inc(x1_made, 1)
                            dve.wait_ge(x1_made, b + 1)
                            norm_stats(x1[0:B, a, :], 0, stats1_made, mv1_made)
                            normalize(z[0:B, a, :], x1[0:B, a, :], 0, sd1_made, rstd1_made, z1_made)
                            norm_stats(z[0:B, a, :], 1, stats2_made, mv2_made)
                            normalize(z[0:B, a, :], z[0:B, a, :], 1, sd2_made, rstd2_made, z2_made)

                        def router():
                            dve.wait_ge(scored, b + 1)
                            dve.tensor_tensor(logits[0:B, :], psS[0:B, SCORE:SCORE + NX], brs[0:B, :], ALU.add)\
                                .then_inc(logits_out, 1)
                            dve.wait_ge(logits_out, b + 1)
                            dve.nop(nofuse=True)
                            dve.max(top8[0:B, :], logits[0:B, :]).then_inc(top_made, 1)
                            dve.wait_ge(top_made, b + 1)
                            dve.tensor_tensor(pair[0:B, 0:1], top8[0:B, 0:1], top8[0:B, 1:2], ALU.subtract)\
                                .then_inc(gap_made, 1)
                            dve.nop(nofuse=True)
                            dve.max_index(top_idx[0:B, :], top8[0:B, :], logits[0:B, :]).then_inc(idx_made, 1)
                            dve.wait_ge(idx_made, b + 1)
                            dve.tensor_copy(top8f[0:B, :], top_idx[0:B, :]).then_inc(idxf_made, 1)

                        def gates():
                            dve.wait_ge(tanh_made, b + 1)
                            dve.tensor_scalar(pair[0:B, 2:3], pair[0:B, 1:2], 0.5, 0.5, ALU.mult, ALU.add)
                            dve.tensor_scalar(pair[0:B, 3:4], pair[0:B, 1:2], -0.5, 0.5, ALU.mult, ALU.add)\
                                .then_inc(share_made, 1)
                            dve.wait_ge(share_made, b + 1)
                            dve.wait_ge(idxf_made, b + 1)
                            dve.tensor_scalar(pick1[0:B, :], iota[0:B, 0:NX], top8f[0:B, 0:1], pair[0:B, 2:3],
                                              ALU.is_equal, ALU.mult)
                            dve.tensor_scalar(w_full[0:B, a, :], iota[0:B, 0:NX], top8f[0:B, 1:2], pair[0:B, 3:4],
                                              ALU.is_equal, ALU.mult).then_inc(pick_made, 1)
                            dve.wait_ge(pick_made, b + 1)
                            dve.tensor_tensor(w_full[0:B, a, :], w_full[0:B, a, :], pick1[0:B, :], ALU.add)\
                                .then_inc(gates_made, 1)

                        def copy_gates():
                            dve.wait_ge(gates_turned, b + 1)
                            dve.tensor_copy(wfT[:, :], psS[0:NX, GATE:GATE + B]).then_inc(gatesT_out, 1)

                        if front:
                            two_norms()
                        if back:
                            for e in range(NX):
                                if e % 2 == 0:
                                    edge_group(e // 2)
                                add_expert(e)
                                if front:
                                    if e == 4:
                                        router()
                                    if e == 5:
                                        gates()
                                    if e == 6:
                                        copy_gates()
                        elif front:
                            for q in range(BG):
                                edge_group(q)
                            router()
                            gates()
                            copy_gates()
                        if front:
                            dve.wait_ge(bias_mixed, b + 1)
                            wait_later(dve, stored[a], (b - a) * 8)
                            dve.tensor_tensor(acc[0:B, a, :], psG[0:B, 0:D], x1[0:B, a, :], ALU.add).then_inc(acc_made, 1)
                    if edges:
                        weigh(dve, 0, 0)
                    run(dve, step, lead)

        with nc.If(too_late > 0):
            with nc.Fori(0, more_rounds + 1):
                edge_pass(xn0_rows)
                shift_windows(False)
            shift_windows(True)
            rows_pass(False)
            with nc.Fori(0, more_rounds + 1):
                edge_pass(hop1_rows)
                shift_windows(False)
            dense(False)
            nc.all_engine_barrier()
        with nc.Else():
            rows_pass(True)
            nc.all_engine_barrier(sems_to_clear=hop_sems)
            dense(True)
            nc.all_engine_barrier()


_INS = ["x", "src", "dst", "edge_weight", "L0_gnn_W", "L0_gnn_b", "L0_ffn_gamma", "L0_ffn_beta", "L0_ffn_Wr",
        "L0_ffn_br", "L0_ffn_W1", "L0_ffn_b1", "L0_ffn_W2", "L0_ffn_b2"]


def kernel(**inputs):
    import numpy as np
    import concourse.bacc as bacc
    from concourse.bass_utils import run_bass_kernel_spmd

    nc = bacc.Bacc("TRN2", target_bir_lowering=False, num_devices=1)
    arrays, args = {}, []
    for name in _INS:
        a = np.ascontiguousarray(inputs[name])
        arrays[f"in_{name}"] = a
        args.append(nc.dram_tensor(f"in_{name}", a.shape, mybir.dt.from_np(a.dtype), kind="ExternalInput").ap())
    out = nc.dram_tensor("out_rows", inputs["x"].shape, F32, kind="ExternalOutput").ap()
    build(nc, *args, out)
    r = run_bass_kernel_spmd(nc, [arrays], core_ids=[0])
    return r.results[0]["out_rows"]
```
